# Optimizing a Trainium2 kernel written in Bass

```python
import numpy as np
import jax
import jax.numpy as jnp

def _softmax(x, axis=-1):
    return jax.nn.softmax(x, axis=axis)

def _gelu(x):
    return jax.nn.gelu(x, approximate=True)

def _silu(x):
    return jax.nn.silu(x)

def _sigmoid(x):
    return jax.nn.sigmoid(x)

def _layernorm(x, axis=-1, eps=1e-05):
    m = jnp.mean(x, axis=axis, keepdims=True)
    v = jnp.var(x, axis=axis, keepdims=True)
    return (x - m) / jnp.sqrt(v + eps)

def _scatter_add(tgt, idx, src, axis=0):
    return tgt.at[idx].add(src)

def _segment_sum(src, seg, n):
    return jax.ops.segment_sum(src, seg, n)
kernel_name = 'mk_dlrm_tower_d1_rec_r8_5f7763'

def setup_inputs(seed: int=0):
    np.random.seed(seed)
    _w = jnp.asarray

    def _rec_inputs():
        import jax
        import jax.numpy as jnp
        _tk = jax.random.key(seed)
        ids = jnp.stack([jax.random.randint(jax.random.fold_in(_tk, 200 + f), (512,), 0, v, jnp.int32) for f, v in enumerate([125000, 12500, 1000, 12500, 1000, 12500, 12500, 12500, 1000, 1000, 12500, 12500, 12500, 12500, 1000, 1000, 1250, 1250, 1250, 1000, 1000, 1250, 1000, 1000, 1000, 1000])], axis=1)
        tbl_0 = 0.05 * jax.random.normal(jax.random.fold_in(_tk, 500 + 0), (125000, 128), jnp.float32)
        tbl_1 = 0.05 * jax.random.normal(jax.random.fold_in(_tk, 500 + 1), (12500, 128), jnp.float32)
        tbl_2 = 0.05 * jax.random.normal(jax.random.fold_in(_tk, 500 + 2), (1000, 128), jnp.float32)
        tbl_3 = 0.05 * jax.random.normal(jax.random.fold_in(_tk, 500 + 3), (12500, 128), jnp.float32)
        tbl_4 = 0.05 * jax.random.normal(jax.random.fold_in(_tk, 500 + 4), (1000, 128), jnp.float32)
        tbl_5 = 0.05 * jax.random.normal(jax.random.fold_in(_tk, 500 + 5), (12500, 128), jnp.float32)
        tbl_6 = 0.05 * jax.random.normal(jax.random.fold_in(_tk, 500 + 6), (12500, 128), jnp.float32)
        tbl_7 = 0.05 * jax.random.normal(jax.random.fold_in(_tk, 500 + 7), (12500, 128), jnp.float32)
        tbl_8 = 0.05 * jax.random.normal(jax.random.fold_in(_tk, 500 + 8), (1000, 128), jnp.float32)
        tbl_9 = 0.05 * jax.random.normal(jax.random.fold_in(_tk, 500 + 9), (1000, 128), jnp.float32)
        tbl_10 = 0.05 * jax.random.normal(jax.random.fold_in(_tk, 500 + 10), (12500, 128), jnp.float32)
        tbl_11 = 0.05 * jax.random.normal(jax.random.fold_in(_tk, 500 + 11), (12500, 128), jnp.float32)
        tbl_12 = 0.05 * jax.random.normal(jax.random.fold_in(_tk, 500 + 12), (12500, 128), jnp.float32)
        tbl_13 = 0.05 * jax.random.normal(jax.random.fold_in(_tk, 500 + 13), (12500, 128), jnp.float32)
        tbl_14 = 0.05 * jax.random.normal(jax.random.fold_in(_tk, 500 + 14), (1000, 128), jnp.float32)
        tbl_15 = 0.05 * jax.random.normal(jax.random.fold_in(_tk, 500 + 15), (1000, 128), jnp.float32)
        tbl_16 = 0.05 * jax.random.normal(jax.random.fold_in(_tk, 500 + 16), (1250, 128), jnp.float32)
        tbl_17 = 0.05 * jax.random.normal(jax.random.fold_in(_tk, 500 + 17), (1250, 128), jnp.float32)
        tbl_18 = 0.05 * jax.random.normal(jax.random.fold_in(_tk, 500 + 18), (1250, 128), jnp.float32)
        tbl_19 = 0.05 * jax.random.normal(jax.random.fold_in(_tk, 500 + 19), (1000, 128), jnp.float32)
        tbl_20 = 0.05 * jax.random.normal(jax.random.fold_in(_tk, 500 + 20), (1000, 128), jnp.float32)
        tbl_21 = 0.05 * jax.random.normal(jax.random.fold_in(_tk, 500 + 21), (1250, 128), jnp.float32)
        tbl_22 = 0.05 * jax.random.normal(jax.random.fold_in(_tk, 500 + 22), (1000, 128), jnp.float32)
        tbl_23 = 0.05 * jax.random.normal(jax.random.fold_in(_tk, 500 + 23), (1000, 128), jnp.float32)
        tbl_24 = 0.05 * jax.random.normal(jax.random.fold_in(_tk, 500 + 24), (1000, 128), jnp.float32)
        tbl_25 = 0.05 * jax.random.normal(jax.random.fold_in(_tk, 500 + 25), (1000, 128), jnp.float32)
        _rk = jax.random.fold_in(_tk, 7)
        r_dense = -0.000520686 + 1.00062 * jax.random.normal(jax.random.fold_in(_rk, 101), (512, 128), jnp.float32)
        W_top1 = 0.0456912 * jax.random.normal(jax.random.fold_in(_tk, 801), (479, 512), jnp.float32)
        W_top2 = 0.0441942 * jax.random.normal(jax.random.fold_in(_tk, 802), (512, 256), jnp.float32)
        W_top3 = 0.0625 * jax.random.normal(jax.random.fold_in(_tk, 803), (256, 1), jnp.float32)
        b_top1 = jnp.zeros((512,), jnp.float32)
        b_top2 = jnp.zeros((256,), jnp.float32)
        return (r_dense, ids, tbl_0, tbl_1, tbl_2, tbl_3, tbl_4, tbl_5, tbl_6, tbl_7, tbl_8, tbl_9, tbl_10, tbl_11, tbl_12, tbl_13, tbl_14, tbl_15, tbl_16, tbl_17, tbl_18, tbl_19, tbl_20, tbl_21, tbl_22, tbl_23, tbl_24, tbl_25, W_top1, b_top1, W_top2, b_top2, W_top3)
    r_dense, ids, tbl_0, tbl_1, tbl_2, tbl_3, tbl_4, tbl_5, tbl_6, tbl_7, tbl_8, tbl_9, tbl_10, tbl_11, tbl_12, tbl_13, tbl_14, tbl_15, tbl_16, tbl_17, tbl_18, tbl_19, tbl_20, tbl_21, tbl_22, tbl_23, tbl_24, tbl_25, W_top1, b_top1, W_top2, b_top2, W_top3 = _rec_inputs()

    def _L0_rec_setup():
        import jax, jax.numpy as jnp
        import numpy as np
        B, NUM_EMBS, D = (2048, 26, 128)
        key = jax.random.key(seed)
        k1, k2 = jax.random.split(key)
        dense = jax.random.normal(k1, (B, D), dtype=jnp.float32)
        embs = jax.random.normal(k2, (B, NUM_EMBS, D), dtype=jnp.float32)
        return {'dense': dense, 'embs': embs}
    _L0_rec_all = _L0_rec_setup()
    _L0_rec_in = {k: v for k, v in _L0_rec_all.items() if k in ()}
    del _L0_rec_all
    return {'r_dense': r_dense, 'ids': ids, 'tbl_0': tbl_0, 'tbl_1': tbl_1, 'tbl_2': tbl_2, 'tbl_3': tbl_3, 'tbl_4': tbl_4, 'tbl_5': tbl_5, 'tbl_6': tbl_6, 'tbl_7': tbl_7, 'tbl_8': tbl_8, 'tbl_9': tbl_9, 'tbl_10': tbl_10, 'tbl_11': tbl_11, 'tbl_12': tbl_12, 'tbl_13': tbl_13, 'tbl_14': tbl_14, 'tbl_15': tbl_15, 'tbl_16': tbl_16, 'tbl_17': tbl_17, 'tbl_18': tbl_18, 'tbl_19': tbl_19, 'tbl_20': tbl_20, 'tbl_21': tbl_21, 'tbl_22': tbl_22, 'tbl_23': tbl_23, 'tbl_24': tbl_24, 'tbl_25': tbl_25, 'W_top1': W_top1, 'b_top1': b_top1, 'W_top2': W_top2, 'b_top2': b_top2, 'W_top3': W_top3}

def reference(r_dense, ids, tbl_0, tbl_1, tbl_2, tbl_3, tbl_4, tbl_5, tbl_6, tbl_7, tbl_8, tbl_9, tbl_10, tbl_11, tbl_12, tbl_13, tbl_14, tbl_15, tbl_16, tbl_17, tbl_18, tbl_19, tbl_20, tbl_21, tbl_22, tbl_23, tbl_24, tbl_25, W_top1, b_top1, W_top2, b_top2, W_top3):
    import jax
    import jax.numpy as jnp

    def _L0_rec_ref(dense, embs):
        import jax, jax.numpy as jnp
        import numpy as np
        B, NUM_EMBS, D = (2048, 26, 128)
        T = jnp.concatenate([dense[:, None, :], embs], axis=1)
        N = T.shape[1]
        Z = jnp.einsum('bnd,bmd->bnm', T, T)
        iu0, iu1 = jnp.triu_indices(N, k=1)
        return Z[:, iu0, iu1]
    e = jnp.stack([tbl_0[ids[:, 0]], tbl_1[ids[:, 1]], tbl_2[ids[:, 2]], tbl_3[ids[:, 3]], tbl_4[ids[:, 4]], tbl_5[ids[:, 5]], tbl_6[ids[:, 6]], tbl_7[ids[:, 7]], tbl_8[ids[:, 8]], tbl_9[ids[:, 9]], tbl_10[ids[:, 10]], tbl_11[ids[:, 11]], tbl_12[ids[:, 12]], tbl_13[ids[:, 13]], tbl_14[ids[:, 14]], tbl_15[ids[:, 15]], tbl_16[ids[:, 16]], tbl_17[ids[:, 17]], tbl_18[ids[:, 18]], tbl_19[ids[:, 19]], tbl_20[ids[:, 20]], tbl_21[ids[:, 21]], tbl_22[ids[:, 22]], tbl_23[ids[:, 23]], tbl_24[ids[:, 24]], tbl_25[ids[:, 25]]], axis=1)
    z = _L0_rec_ref(r_dense, e)
    z = z.reshape(z.shape[0], -1)
    h = jnp.concatenate([z, r_dense], axis=1)
    h = jnp.maximum(h @ W_top1 + b_top1, 0.0)
    h = jnp.maximum(h @ W_top2 + b_top2, 0.0)
    y = h @ W_top3
    return y

_drawn_inputs = setup_inputs


def setup_inputs(seed=0):
    import zlib

    import numpy as np

    out = dict(_drawn_inputs(seed))
    spreads = {'b_top1': (0.0, 0.1), 'b_top2': (0.0, 0.1)}
    factors = {}
    for name, (base, spread) in spreads.items():
        noise = np.random.default_rng([zlib.crc32(name.encode()), seed]).standard_normal(out[name].shape)
        drawn = base * np.exp(spread * noise) if base else spread * noise
        out[name] = jnp.asarray(drawn.astype(out[name].dtype))
    for name, factor in factors.items():
        out[name] = (out[name] * factor).astype(out[name].dtype)
    return out
```

```python
import concourse.bass as bass
from concourse import mybir
from contextlib import ExitStack

BATCH = 512
TABLES = 26
DIM = 128
VECTORS = TABLES + 1
HIDDEN1, HIDDEN2 = 512, 256
PAIRS = VECTORS * (VECTORS - 1) // 2

TILE = 128
TILES = BATCH // TILE
QUADS = 4
QUAD = 32
GROUPS = TILE // QUADS
HALF_CYCLE = (VECTORS - 1) // 2
FOLDED = HALF_CYCLE + 1
SLABS = -(-FOLDED // QUADS)
K1 = SLABS + 1
CHUNKS1, CHUNKS2 = HIDDEN1 // 128, HIDDEN2 // 128

GATHERED = list(range(TABLES))
NG = len(GATHERED)
ORDER = [0] + [f + 1 for f in GATHERED]
KEPT = 1
GROUP = 4
SETS = [list(range(a, min(a + GROUP, NG))) for a in range(0, NG, GROUP)]
ACT_SETS, DVE_SETS = (len(SETS) + 1) // 2, len(SETS) // 2
ID_CUT = GROUP * (len(SETS) // 2)
ID_PARTS = [(0, ID_CUT), (ID_CUT, NG)]


def slab_columns(s):
    return (FOLDED - s + QUADS - 1) // QUADS


def build(nc, dense, ids, tables, w1, w2, b2, w3, keep_low, y):
    fp32, i32 = mybir.dt.float32, mybir.dt.int32
    ALU = mybir.AluOpType
    ACT = mybir.ActivationFunctionType

    with ExitStack() as ctx:
        def sb(name, shape, dt=fp32):
            return ctx.enter_context(nc.sbuf_tensor(name, shape, dt))

        def ps(name, shape):
            return ctx.enter_context(nc.psum_tensor(name, shape, fp32))

        def sem(name):
            return ctx.enter_context(nc.semaphore(name))

        identity = sb("identity", [128, 128])
        id_part = [sb(f"id_part{h}", [TILE, b - a], i32) for h, (a, b) in enumerate(ID_PARTS)]
        dense_rows = sb("dense_rows", [TILE, TILES, DIM])
        rows = sb("rows", [TILE, NG, DIM])
        kept = sb("kept", [DIM, KEPT, BATCH])
        vectors = sb("vectors", [DIM, TILE, VECTORS])
        folded = sb("folded", [128, FOLDED, GROUPS])
        pairs = sb("pairs", [128, SLABS, TILE])
        keep_low_sb = sb("keep_low_sb", [128, FOLDED - 1], i32)
        w1_sb = sb("w1_sb", [128, K1, HIDDEN1])
        w2_sb = sb("w2_sb", [128, CHUNKS1, HIDDEN2])
        b2_sb = sb("b2_sb", [128, CHUNKS2])
        w3_sb = sb("w3_sb", [128, CHUNKS2])
        h1 = sb("h1", [128, CHUNKS1, TILE])
        h2 = sb("h2", [128, CHUNKS2, TILE])
        y_sb = sb("y_sb", [1, BATCH])

        turned = [ps(f"turned{i}", [DIM, GROUP, TILE]) for i in range(2)]
        gram = ps("gram", [128, 2, GROUPS // 2, 32])
        kept_ps = ps("kept_ps", [DIM, BATCH])
        h1_ps = ps("h1_ps", [128, CHUNKS1, TILE])
        h2_ps = ps("h2_ps", [128, 4, TILE])
        y_ps = h2_ps[0:1, CHUNKS2, :]

        s_ids = [sem(f"s_ids{h}") for h in range(2)]
        s_dense = sem("s_dense")
        s_mask = sem("s_mask")
        s_w1 = sem("s_w1")
        s_w2 = sem("s_w2")
        s_b2 = sem("s_b2")
        s_w3 = sem("s_w3")
        s_out = sem("s_out")
        s_gathered = [sem(f"s_gathered{k}") for k in range(len(SETS))]
        s_identity = sem("s_identity")
        s_pairs_init = sem("s_pairs_init")
        s_gram_zero = sem("s_gram_zero")
        s_kept_ps = sem("s_kept_ps")
        s_kept = sem("s_kept")
        s_turned = sem("s_turned")
        s_vec_act = sem("s_vec_act")
        s_vec_dve = sem("s_vec_dve")
        s_vec_kept = sem("s_vec_kept")
        s_gram = sem("s_gram")
        s_low = sem("s_low")
        s_folded = sem("s_folded")
        s_pairs_act = sem("s_pairs_act")
        s_pairs_dve = sem("s_pairs_dve")
        s_h1_ps = sem("s_h1_ps")
        s_h1 = sem("s_h1")
        s_h2_ps = sem("s_h2_ps")
        s_h2 = sem("s_h2")
        s_y_ps = sem("s_y_ps")
        s_y = sem("s_y")

        block = ctx.enter_context(nc.Block())

        @block.sync
        def _(sp):
            for h, (a, b) in enumerate(ID_PARTS):
                sp.dma_start(id_part[h][:], ids[0, :, a:b]).then_inc(s_ids[h], 16)
            sp.dma_start(keep_low_sb[:], keep_low).then_inc(s_mask, 16)
            sp.dma_start(w1_sb[:], w1).then_inc(s_w1, 16)
            sp.dma_start(w2_sb[:], w2.rearrange("(k p) n -> p k n", p=128)).then_inc(s_w2, 16)
            sp.dma_start(b2_sb[:], b2).then_inc(s_b2, 16)
            sp.dma_start(w3_sb[:], w3).then_inc(s_w3, 16)
            with sp.Fori(1, TILES) as t:
                for h, (a, b) in enumerate(ID_PARTS):
                    sp.wait_ge(s_ids[h], 16)
                    for k, members in enumerate(SETS):
                        if a <= members[0] < b:
                            sp.wait_ge(s_gathered[k], t * (16 * len(members)))
                    sp.dma_start(id_part[h][:], ids[bass.ds(t, 1), :, a:b].rearrange("o p f -> (o p) f"))\
                      .then_inc(s_ids[h], 16)
            sp.wait_ge(s_y, TILES)
            sp.dma_start(y.rearrange("b o -> o b"), y_sb[:]).then_inc(s_out, 16)
            sp.wait_ge(s_out, 16)

        @block.gpsimd
        def _(pool):
            pool.memset(identity[:], 0.0).then_inc(s_identity, 1)
            pool.wait_ge(s_identity, 1)
            pool.affine_select(out=identity[:], in_=identity[:], compare_op=ALU.not_equal, fill=1.0, base=0,
                               pattern=[[-1, 128]], channel_multiplier=1).then_inc(s_identity, 1)
            pool.memset(pairs[:], 0.0).then_inc(s_pairs_init, 1)
            pool.wait_ge(s_pairs_init, 1)
            pool.affine_select(out=pairs[:, 0, :], in_=pairs[:, 0, :], compare_op=ALU.not_equal, fill=1.0,
                               base=-VECTORS, pattern=[[0, TILE]], channel_multiplier=1).then_inc(s_pairs_init, 1)

            sets_read = pool.alloc_register("sets_read")
            pool.reg_mov(sets_read, 1)

            def gather_tile(t, first):
                for h, (a, b) in enumerate(ID_PARTS):
                    pool.wait_ge(s_ids[h], t * 16 + 16)
                    for k, members in enumerate(SETS):
                        if not a <= members[0] < b:
                            continue
                        if not first:
                            pool.wait_ge(s_turned, sets_read)
                            pool.reg_add(sets_read, sets_read, 1)
                        for g in members:
                            pool.indirect_dma_start(rows[:, g, :], None, tables[GATHERED[g]],
                                                    bass.IndirectOffsetOnAxis(id_part[h][:, g - a:g - a + 1], 0))\
                                .then_inc(s_gathered[k], 16)

            gather_tile(0, first=True)
            with pool.Fori(1, TILES) as t:
                gather_tile(t, first=False)

        @block.tensor
        def _(pe):
            def turn_set(t, k, first):
                members = SETS[k]
                pe.wait_ge(s_gathered[k], t * (16 * len(members)) + 16 * len(members))
                evacuated, per_tile = (s_vec_dve, DVE_SETS) if k % 2 else (s_vec_act, ACT_SETS)
                if not first or k >= 2:
                    pe.wait_ge(evacuated, t * per_tile + k // 2)
                for i, g in enumerate(members):
                    last = pe.transpose(turned[k % 2][:, i, :], rows[:, g, :], identity[:])
                last.then_inc(s_turned, 1)

            def layer1(t):
                pe.wait_ge(s_pairs_act, t + 1)
                pe.wait_ge(s_pairs_dve, t + 1)
                for c in range(CHUNKS1):
                    for k in range(SLABS):
                        pe.matmul(h1_ps[:, c, :], w1_sb[:, k, c * 128:c * 128 + 128], pairs[:, k, :],
                                  start=(k == 0), stop=False)
                    last = pe.matmul(h1_ps[:, c, :], w1_sb[:, SLABS, c * 128:c * 128 + 128],
                                     kept[:, 0, bass.ds(t * TILE, TILE)], start=False, stop=True)
                last.then_inc(s_h1_ps, 1)

            def layer2(t):
                pe.wait_ge(s_h1, t + 1)
                for c in range(CHUNKS2):
                    for k in range(CHUNKS1):
                        last = pe.matmul(h2_ps[:, c, :], w2_sb[:, k, c * 128:c * 128 + 128], h1[:, k, :],
                                         start=(k == 0), stop=(k == CHUNKS1 - 1))
                last.then_inc(s_h2_ps, 1)

            def layer3(t):
                pe.wait_ge(s_h2, t + 1)
                for k in range(CHUNKS2):
                    last = pe.matmul(y_ps, w3_sb[:, k:k + 1], h2[:, k, :], start=(k == 0), stop=(k == CHUNKS2 - 1))
                last.then_inc(s_y_ps, 1)

            def gram_tile(t, first):
                pe.wait_ge(s_vec_act, t * ACT_SETS + ACT_SETS)
                pe.wait_ge(s_vec_dve, t * DVE_SETS + DVE_SETS)
                pe.wait_ge(s_vec_kept, t + 1)
                if not first:
                    pe.wait_ge(s_folded, t)
                for g in range(GROUPS):
                    for q in range(QUADS):
                        v = vectors[:, q * GROUPS + g, :]
                        last = pe.matmul(gram[q * QUAD:q * QUAD + VECTORS, g // 16, g % 16, 0:VECTORS], v, v,
                                         start=True, stop=True)
                last.then_inc(s_gram, 1)

            pe.wait_ge(s_identity, 2)
            pe.wait_ge(s_dense, 16)
            for j in range(TILES):
                last = pe.transpose(kept_ps[:, j * TILE:j * TILE + TILE], dense_rows[:, j, :], identity[:])
            last.then_inc(s_kept_ps, 1)

            for k in range(len(SETS)):
                turn_set(0, k, first=True)
            pe.wait_ge(s_gram_zero, 1)
            gram_tile(0, first=True)
            pe.wait_ge(s_w1, 16)
            pe.wait_ge(s_w2, 16)
            pe.wait_ge(s_w3, 16)
            with pe.Fori(1, TILES) as t:
                turn_set(t, 0, first=False)
                turn_set(t, 1, first=False)
                turn_set(t, 2, first=False)
                layer1(t - 1)
                turn_set(t, 3, first=False)
                layer2(t - 1)
                turn_set(t, 4, first=False)
                layer3(t - 1)
                for k in range(5, len(SETS)):
                    turn_set(t, k, first=False)
                gram_tile(t, first=False)
            layer1(TILES - 1)
            layer2(TILES - 1)
            layer3(TILES - 1)

        def set_columns(k):
            a = KEPT + SETS[k][0]
            return vectors[:, :, a:a + len(SETS[k])].rearrange("p b v -> p v b")

        def move(copy, s, q):
            n = slab_columns(s)
            return copy(pairs[s * QUAD:s * QUAD + VECTORS, 0:n, q * GROUPS:q * GROUPS + GROUPS],
                        folded[q * QUAD:q * QUAD + VECTORS, s:FOLDED:QUADS, :])

        ACT_MOVES = [(s, q) for s in range(QUADS) for q in (0, 1)]
        DVE_MOVES = [(s, q) for s in range(QUADS) for q in (2, 3)]

        @block.scalar
        def _(act):
            act.dma_start(dense_rows[:], dense.rearrange("(j p) d -> p j d", p=TILE)).then_inc(s_dense, 16)

            def take_set(t, k):
                act.wait_ge(s_turned, t * len(SETS) + k + 1)
                act.copy(set_columns(k), turned[0][:, 0:len(SETS[k]), :]).then_inc(s_vec_act, 1)

            def take_kept(t, first):
                if not first:
                    act.wait_ge(s_gram, t)
                act.copy(vectors[:, :, 0:KEPT].rearrange("p b v -> p v b"),
                         kept[:, :, bass.ds(t * TILE, TILE)]).then_inc(s_vec_kept, 1)

            def move_pairs(t, first):
                act.wait_ge(s_folded, t + 1)
                if not first:
                    act.wait_ge(s_h1_ps, t)
                for s, q in ACT_MOVES:
                    last = move(act.copy, s, q)
                last.then_inc(s_pairs_act, 1)

            def relu1(t):
                act.wait_ge(s_h1_ps, t + 1)
                act.activation(h1[:], h1_ps[:], ACT.Relu).then_inc(s_h1, 1)

            def relu2(t):
                act.wait_ge(s_h2_ps, t + 1)
                for c in range(CHUNKS2):
                    last = act.activation(h2[:, c, :], h2_ps[:, c, :], ACT.Relu, bias=b2_sb[:, c:c + 1])
                last.then_inc(s_h2, 1)

            act.wait_ge(s_kept_ps, 1)
            act.copy(kept[:, 0, :], kept_ps[:]).then_inc(s_kept, 1)
            act.wait_ge(s_kept, 1)
            take_kept(0, first=True)
            for k in range(0, len(SETS), 2):
                take_set(0, k)
            act.wait_ge(s_pairs_init, 2)
            move_pairs(0, first=True)
            act.wait_ge(s_b2, 16)
            with act.Fori(1, TILES) as t:
                take_kept(t, first=False)
                take_set(t, 0)
                take_set(t, 2)
                relu1(t - 1)
                relu2(t - 1)
                take_set(t, 4)
                for k in range(6, len(SETS), 2):
                    take_set(t, k)
                move_pairs(t, first=False)
            relu1(TILES - 1)
            relu2(TILES - 1)

        @block.vector
        def _(dve):
            dve.memset(gram[:], 0.0).then_inc(s_gram_zero, 1)

            def take_set(t, k):
                dve.wait_ge(s_turned, t * len(SETS) + k + 1)
                dve.tensor_copy(set_columns(k), turned[1][:, 0:len(SETS[k]), :]).then_inc(s_vec_dve, 1)

            def fold(t, first):
                dve.wait_ge(s_gram, t + 1)
                if not first:
                    dve.wait_ge(s_pairs_act, t)
                whole = folded[:].rearrange("p c (h g) -> p c h g", h=2)
                low = gram[:].rearrange("p h g c -> p c h g")
                dve.tensor_copy(whole, low[:, HALF_CYCLE:VECTORS]).then_inc(s_low, 1)
                dve.wait_ge(s_mask, 16)
                dve.wait_ge(s_low, t + 1)
                dve.copy_predicated(whole[:, 0:HALF_CYCLE],
                                    keep_low_sb[:].unsqueeze(2).unsqueeze(3)
                                    .to_broadcast([128, HALF_CYCLE, 2, GROUPS // 2]),
                                    low[:, 0:HALF_CYCLE]).then_inc(s_folded, 1)

            def move_pairs(t, first):
                dve.wait_ge(s_folded, t + 1)
                if not first:
                    dve.wait_ge(s_h1_ps, t)
                for s, q in DVE_MOVES:
                    last = move(dve.tensor_copy, s, q)
                last.then_inc(s_pairs_dve, 1)

            def take_y(t):
                dve.wait_ge(s_y_ps, t + 1)
                dve.tensor_copy(y_sb[:, bass.ds(t * TILE, TILE)], y_ps).then_inc(s_y, 1)

            for k in range(1, len(SETS), 2):
                take_set(0, k)
            fold(0, first=True)
            dve.wait_ge(s_pairs_init, 2)
            move_pairs(0, first=True)
            with dve.Fori(1, TILES) as t:
                take_set(t, 1)
                take_set(t, 3)
                take_y(t - 1)
                for k in range(5, len(SETS), 2):
                    take_set(t, k)
                fold(t, first=False)
                move_pairs(t, first=False)
            take_y(TILES - 1)


def kernel(**inputs):
    import numpy as np
    import concourse.bacc as bacc
    from concourse.bass_utils import run_bass_kernel_spmd

    w_top1 = np.asarray(inputs["W_top1"])
    w1 = np.zeros((128, K1, HIDDEN1), w_top1.dtype)
    keep_low = np.zeros((128, HALF_CYCLE), np.int32)
    for c in range(FOLDED):
        s, k = c % QUADS, c // QUADS
        for n in range(VECTORS):
            for m in (c, c + HALF_CYCLE):
                if c == HALF_CYCLE and m == c:
                    continue
                if 1 <= (m - n) % VECTORS <= HALF_CYCLE:
                    a, b = sorted((ORDER[n], ORDER[m]))
                    w1[s * QUAD + n, k] = w_top1[a * VECTORS - a * (a + 1) // 2 + b - a - 1]
                    if m == c:
                        for q in range(QUADS):
                            keep_low[q * QUAD + n, c] = 1
    w1[VECTORS, 0] = np.asarray(inputs["b_top1"])
    w1[:, SLABS] = w_top1[PAIRS:]

    arrays = {
        "dense": np.asarray(inputs["r_dense"]),
        "ids": np.ascontiguousarray(np.asarray(inputs["ids"])[:, GATHERED].reshape(TILES, TILE, NG)),
        "w1": w1,
        "w2": np.asarray(inputs["W_top2"]),
        "b2": np.ascontiguousarray(np.asarray(inputs["b_top2"]).reshape(CHUNKS2, 128).T),
        "w3": np.ascontiguousarray(np.asarray(inputs["W_top3"]).reshape(CHUNKS2, 128).T),
        "keep_low": keep_low,
    }
    for f in range(TABLES):
        arrays[f"table{f}"] = np.asarray(inputs[f"tbl_{f}"])

    nc = bacc.Bacc("TRN2", target_bir_lowering=False, num_devices=1)
    ins = {n: nc.dram_tensor(n, a.shape, mybir.dt.from_np(a.dtype), kind="ExternalInput").ap()
           for n, a in arrays.items()}
    y = nc.dram_tensor("y", (BATCH, 1), mybir.dt.float32, kind="ExternalOutput").ap()
    build(nc, ins["dense"], ins["ids"], [ins[f"table{f}"] for f in range(TABLES)],
          ins["w1"], ins["w2"], ins["b2"], ins["w3"], ins["keep_low"], y)
    return run_bass_kernel_spmd(nc, [arrays], core_ids=[0]).results[0]["y"]
```

```python
import concourse.bass as bass
from concourse import mybir
from contextlib import ExitStack

BATCH = 512
TABLES = 26
DIM = 128
VECTORS = TABLES + 1
HIDDEN1, HIDDEN2 = 512, 256
PAIRS = VECTORS * (VECTORS - 1) // 2

TILE = 128
TILES = BATCH // TILE
QUADS = 4
QUAD = 32
GROUPS = TILE // QUADS
HALF = GROUPS // 2
HALF_CYCLE = (VECTORS - 1) // 2
FOLDED = HALF_CYCLE + 1
SLABS = -(-FOLDED // QUADS)
K1 = SLABS + 1
CHUNKS1, CHUNKS2 = HIDDEN1 // 128, HIDDEN2 // 128

ROWS = [125000, 12500, 1000, 12500, 1000, 12500, 12500, 12500, 1000, 1000, 12500, 12500, 12500, 12500,
        1000, 1000, 1250, 1250, 1250, 1000, 1000, 1250, 1000, 1000, 1000, 1000]
EARLY, LATE = 3, 7
LOOKUPS = EARLY + LATE
LOOKED_UP = [f for f in range(TABLES) if ROWS[f] == min(ROWS)][:LOOKUPS]
GATHERED = [f for f in range(TABLES) if f not in LOOKED_UP]
NG = len(GATHERED)
LOAD_AHEAD = 3
CHUNKS = 8
TABLE_PARTS = min(ROWS) // CHUNKS
ORDER = [0] + [f + 1 for f in LOOKED_UP + GATHERED]
KEPT = 1 + LOOKUPS
GROUP = 4
SETS = [list(range(a, min(a + GROUP, NG))) for a in range(0, NG, GROUP)]
LATE_SETS = [list(range(a, min(a + GROUP, LATE))) for a in range(0, LATE, GROUP)]
ID_CUT = GROUP * (len(SETS) // 2)
ID_PARTS = [(0, ID_CUT), (ID_CUT, NG)]

TILE_STEPS = [("turn", 0), ("turn", 1), ("layer1", 0), ("turn", 2), ("layer2", 0), ("turn", 3), ("layer3", 0),
              ("gram", 0), ("fold", 0)]
FIRST_STEPS = [("look", 0), ("turn", 0), ("look", 1), ("turn", 1), ("look", 2), ("turn", 2), ("look", 3),
               ("turn", 3), ("look", 4), ("late", 0), ("late", 1), ("gram", 0), ("look", 5), ("fold", 0)]
SECOND_STEPS = [("look", 6), ("turn", 0), ("turn", 1), ("look", 7), ("layer1", 0), ("turn", 2), ("look", 8),
                ("layer2", 0), ("turn", 3), ("layer3", 0), ("look", 9), ("gram", 0), ("fold", 0)]
assert [i for step, i in FIRST_STEPS + SECOND_STEPS if step == "look"] == list(range(LOOKUPS))
assert [i for step, i in FIRST_STEPS if step == "late"] == list(range(len(LATE_SETS)))
for steps in (TILE_STEPS, FIRST_STEPS, SECOND_STEPS):
    assert [i for step, i in steps if step == "turn"] == list(range(len(SETS)))


def first_sample(i):
    return 0 if i < EARLY else TILE



def slab_columns(s):
    return (FOLDED - s + QUADS - 1) // QUADS


def build(nc, dense, ids, lookup_ids, late_ids, row_ids, tables, w1, w2, b2, w3, keep_low, y):
    fp32, fp32r, i32 = mybir.dt.float32, mybir.dt.float32r, mybir.dt.int32
    ALU = mybir.AluOpType
    ACT = mybir.ActivationFunctionType

    with ExitStack() as ctx:
        def sb(name, shape, dt=fp32):
            return ctx.enter_context(nc.sbuf_tensor(name, shape, dt))

        def ps(name, shape):
            return ctx.enter_context(nc.psum_tensor(name, shape, fp32))

        def sem(name):
            return ctx.enter_context(nc.semaphore(name))

        identity = sb("identity", [128, 128])
        id_part = [sb(f"id_part{h}", [TILE, b - a], i32) for h, (a, b) in enumerate(ID_PARTS)]
        dense_rows = sb("dense_rows", [TILE, TILES, DIM])
        row_ids_sb = sb("row_ids_sb", [TABLE_PARTS, CHUNKS])
        table_sb = [sb(f"table_sb{i}", [TABLE_PARTS, CHUNKS, DIM]) for i in range(LOOKUPS)]
        ids_sb = [sb(f"ids_sb{i}", [TABLE_PARTS, BATCH], i32) for i in range(LOOKUPS)]
        high = [sb(f"high{i}", [TABLE_PARTS, CHUNKS, DIM], fp32r) for i in range(2)]
        low = [sb(f"low{i}", [TABLE_PARTS, CHUNKS, DIM], fp32r) for i in range(2)]
        onehot = [sb(f"onehot{i}", [TABLE_PARTS, CHUNKS, BATCH], fp32r) for i in range(2)]
        late_id_sb = sb("late_id_sb", [TILE, LATE], i32)
        late_rows = sb("late_rows", [TILE, LATE, DIM])
        rows = sb("rows", [TILE, NG, DIM])
        kept = sb("kept", [DIM, KEPT, BATCH])
        vectors = sb("vectors", [DIM, TILE, VECTORS])
        folded = sb("folded", [128, FOLDED, GROUPS])
        pairs = sb("pairs", [128, SLABS, TILE])
        keep_low_sb = sb("keep_low_sb", [128, FOLDED - 1], i32)
        w1_sb = sb("w1_sb", [128, K1, HIDDEN1])
        w2_sb = sb("w2_sb", [128, CHUNKS1, HIDDEN2])
        b2_sb = sb("b2_sb", [128, CHUNKS2])
        w3_sb = sb("w3_sb", [128, CHUNKS2])
        h1 = sb("h1", [128, CHUNKS1, TILE])
        h2 = sb("h2", [128, CHUNKS2, TILE])
        y_sb = sb("y_sb", [1, BATCH])

        turned = [ps(f"turned{i}", [DIM, GROUP, TILE]) for i in range(2)]
        gram = ps("gram", [128, 2, HALF, 32])
        kept_ps = [ps(f"kept_ps{i}", [DIM, BATCH]) for i in range(2)]
        h1_ps = ps("h1_ps", [128, 4, TILE])
        h2_ps = ps("h2_ps", [128, 4, TILE])
        layer1_last_ps = [h1_ps[:, 0, :], turned[0][:, 0, :], turned[1][:, 0, :], kept_ps[0][:, 0:TILE]]
        layer2_last_ps = [h2_ps[:, 0, :], kept_ps[1][:, 0:TILE]]
        y_ps = h2_ps[0:1, CHUNKS2, :]

        s_ids = [sem(f"s_ids{h}") for h in range(2)]
        s_dense = sem("s_dense")
        s_mask = sem("s_mask")
        s_w1 = sem("s_w1")
        s_w2 = sem("s_w2")
        s_b2 = sem("s_b2")
        s_w3 = sem("s_w3")
        s_out = sem("s_out")
        s_gathered = [sem(f"s_gathered{k}") for k in range(len(SETS))]
        s_identity = sem("s_identity")
        s_pairs_init = sem("s_pairs_init")
        s_gram_zero = sem("s_gram_zero")
        s_row_ids = sem("s_row_ids")
        s_late_ids = sem("s_late_ids")
        s_late_gathered = [sem(f"s_late_gathered{j}") for j in range(len(LATE_SETS))]
        s_late_turned = sem("s_late_turned")
        s_late_vec = sem("s_late_vec")
        s_table = [sem(f"s_table{i}") for i in range(LOOKUPS)]
        s_lookup_ids = [sem(f"s_lookup_ids{i}") for i in range(LOOKUPS)]
        s_high = sem("s_high")
        s_low = sem("s_low")
        s_onehot = sem("s_onehot")
        s_kept_ps = sem("s_kept_ps")
        s_kept = sem("s_kept")
        s_turned = sem("s_turned")
        s_vec = sem("s_vec")
        s_vec_kept = sem("s_vec_kept")
        s_gram = sem("s_gram")
        s_far = sem("s_far")
        s_folded = sem("s_folded")
        s_pairs_act = sem("s_pairs_act")
        s_pairs_dve = sem("s_pairs_dve")
        s_h1_ps = sem("s_h1_ps")
        s_h1_last_ps = sem("s_h1_last_ps")
        s_h2_last_ps = sem("s_h2_last_ps")
        s_h1 = sem("s_h1")
        s_h2_ps = sem("s_h2_ps")
        s_h2 = sem("s_h2")
        s_y_ps = sem("s_y_ps")
        s_y = sem("s_y")

        block = ctx.enter_context(nc.Block())

        @block.sync
        def _(sp):
            def load_ids_of_tile0(h):
                a, b = ID_PARTS[h]
                sp.dma_start(id_part[h][:], ids[0, :, a:b]).then_inc(s_ids[h], 16)

            def load_table(i):
                a = first_sample(i)
                sp.dma_start(table_sb[i][:], tables[LOOKED_UP[i]].rearrange("(p c) d -> p c d", c=CHUNKS))\
                  .then_inc(s_table[i], 16)
                sp.dma_start(ids_sb[i][:, a:], lookup_ids[i:i + 1, a:].partition_broadcast(TABLE_PARTS)
                             .rearrange("p o b -> p (o b)")).then_inc(s_lookup_ids[i], 16)

            load_ids_of_tile0(0)
            load_table(0)
            sp.dma_start(row_ids_sb[:], row_ids).then_inc(s_row_ids, 16)
            load_ids_of_tile0(1)
            sp.dma_start(late_id_sb[:], late_ids).then_inc(s_late_ids, 16)
            for i in range(1, LOOKUPS):
                if LOAD_AHEAD <= i < LOAD_AHEAD + 3:
                    sp.wait_ge(s_low, i - LOAD_AHEAD + 1)
                load_table(i)
            sp.dma_start(keep_low_sb[:], keep_low).then_inc(s_mask, 16)
            with sp.Fori(1, TILES) as t:
                for h, (a, b) in enumerate(ID_PARTS):
                    sp.wait_ge(s_ids[h], 16)
                    for k, members in enumerate(SETS):
                        if a <= members[0] < b:
                            sp.wait_ge(s_gathered[k], t * (16 * len(members)))
                    sp.dma_start(id_part[h][:], ids[bass.ds(t, 1), :, a:b].rearrange("o p f -> (o p) f"))\
                      .then_inc(s_ids[h], 16)
            sp.wait_ge(s_y, TILES)
            sp.dma_start(y.rearrange("b o -> o b"), y_sb[:]).then_inc(s_out, 16)
            sp.wait_ge(s_out, 16)

        @block.gpsimd
        def _(pool):
            pool.memset(identity[:], 0.0).then_inc(s_identity, 1)
            pool.wait_ge(s_identity, 1)
            pool.affine_select(out=identity[:], in_=identity[:], compare_op=ALU.not_equal, fill=1.0, base=0,
                               pattern=[[-1, 128]], channel_multiplier=1).then_inc(s_identity, 1)
            pool.memset(pairs[:], 0.0).then_inc(s_pairs_init, 1)
            pool.wait_ge(s_pairs_init, 1)
            pool.affine_select(out=pairs[:, 0, :], in_=pairs[:, 0, :], compare_op=ALU.not_equal, fill=1.0,
                               base=-VECTORS, pattern=[[0, TILE]], channel_multiplier=1).then_inc(s_pairs_init, 1)

            sets_read = pool.alloc_register("sets_read")
            pool.reg_mov(sets_read, 1)

            def gather_tile(t, first):
                for h, (a, b) in enumerate(ID_PARTS):
                    pool.wait_ge(s_ids[h], t * 16 + 16)
                    for k, members in enumerate(SETS):
                        if not a <= members[0] < b:
                            continue
                        if not first:
                            pool.wait_ge(s_turned, sets_read)
                            pool.reg_add(sets_read, sets_read, 1)
                        for g in members:
                            pool.indirect_dma_start(rows[:, g, :], None, tables[GATHERED[g]],
                                                    bass.IndirectOffsetOnAxis(id_part[h][:, g - a:g - a + 1], 0))\
                                .then_inc(s_gathered[k], 16)

            gather_tile(0, first=True)
            pool.wait_ge(s_late_ids, 16)
            for j, members in enumerate(LATE_SETS):
                for g in members:
                    pool.indirect_dma_start(late_rows[:, g, :], None, tables[LOOKED_UP[EARLY + g]],
                                            bass.IndirectOffsetOnAxis(late_id_sb[:, g:g + 1], 0))\
                        .then_inc(s_late_gathered[j], 16)
            with pool.Fori(1, TILES) as t:
                gather_tile(t, first=False)

        @block.tensor
        def _(pe):
            def turn_set(t, k, first):
                members = SETS[k]
                pe.wait_ge(s_gathered[k], t * (16 * len(members)) + 16 * len(members))
                if not first or k >= 2:
                    pe.wait_ge(s_vec, t * len(SETS) + (k - 1))
                for i, g in enumerate(members):
                    last = pe.transpose(turned[k % 2][:, i, :], rows[:, g, :], identity[:])
                last.then_inc(s_turned, 1)

            def turn_late(j):
                pe.wait_ge(s_late_gathered[j], 16 * len(LATE_SETS[j]))
                n = len(SETS) + j
                pe.wait_ge(s_vec, len(SETS))
                if j >= 2:
                    pe.wait_ge(s_late_vec, j - 1)
                for i, g in enumerate(LATE_SETS[j]):
                    last = pe.transpose(turned[n % 2][:, i, :], late_rows[:, g, :], identity[:])
                last.then_inc(s_late_turned, 1)

            def pairs_ready(t, h):
                pe.wait_ge(s_pairs_act, 2 * t + (h + 1))
                pe.wait_ge(s_pairs_dve, 2 * t + (h + 1))

            def layer1(t):
                pairs_ready(t, 1)
                for c in range(CHUNKS1):
                    for k in range(SLABS):
                        pe.matmul(h1_ps[:, c, :], w1_sb[:, k, c * 128:c * 128 + 128], pairs[:, k, :],
                                  start=(k == 0), stop=False)
                    last = pe.matmul(h1_ps[:, c, :], w1_sb[:, SLABS, c * 128:c * 128 + 128],
                                     kept[:, 0, bass.ds(t * TILE, TILE)], start=False, stop=True)
                last.then_inc(s_h1_ps, 1)

            def layer1_last(t):
                outs = [layer1_last_ps[c] for c in range(CHUNKS1)]
                pe.wait_ge(s_vec, TILES * len(SETS))
                for c in range(CHUNKS1):
                    pe.matmul(outs[c], w1_sb[:, SLABS, c * 128:c * 128 + 128],
                              kept[:, 0, t * TILE:t * TILE + TILE], start=True, stop=False)
                pairs_ready(t, 1)
                for c in range(CHUNKS1):
                    for k in range(SLABS):
                        last = pe.matmul(outs[c], w1_sb[:, k, c * 128:c * 128 + 128], pairs[:, k, :],
                                         start=False, stop=(k == SLABS - 1))
                    last.then_inc(s_h1_last_ps, 1)

            def layer2(t):
                pe.wait_ge(s_h1, t + 1)
                for c in range(CHUNKS2):
                    for k in range(CHUNKS1):
                        last = pe.matmul(h2_ps[:, c, :], w2_sb[:, k, c * 128:c * 128 + 128], h1[:, k, :],
                                         start=(k == 0), stop=(k == CHUNKS1 - 1))
                last.then_inc(s_h2_ps, 1)

            def layer2_last(t):
                for c in range(CHUNKS2):
                    for k in range(CHUNKS1):
                        if c == 0:
                            pe.wait_ge(s_h1, t + (k + 1))
                        last = pe.matmul(layer2_last_ps[c], w2_sb[:, k, c * 128:c * 128 + 128], h1[:, k, :],
                                         start=(k == 0), stop=(k == CHUNKS1 - 1))
                    last.then_inc(s_h2_last_ps, 1)

            def layer3(t, last_tile=False):
                if not last_tile:
                    pe.wait_ge(s_h2, t + 1)
                for k in range(CHUNKS2):
                    if last_tile:
                        pe.wait_ge(s_h2, t + (k + 1))
                    last = pe.matmul(y_ps, w3_sb[:, k:k + 1], h2[:, k, :], start=(k == 0), stop=(k == CHUNKS2 - 1))
                last.then_inc(s_y_ps, 1)

            def gram_tile(t, first):
                pe.wait_ge(s_vec, t * len(SETS) + len(SETS))
                pe.wait_ge(s_vec_kept, t + 1)
                if first:
                    pe.wait_ge(s_late_vec, len(LATE_SETS))
                for g in range(GROUPS):
                    if not first and g % HALF == 0:
                        pe.wait_ge(s_folded, 2 * t + (g // HALF - 1))
                    for q in range(QUADS):
                        v = vectors[:, q * GROUPS + g, :]
                        last = pe.matmul(gram[q * QUAD:q * QUAD + VECTORS, g // HALF, g % HALF, 0:VECTORS], v, v,
                                         start=True, stop=True)
                    if g % HALF == HALF - 1:
                        last.then_inc(s_gram, 1)

            pe.wait_ge(s_identity, 2)
            pe.wait_ge(s_dense, 16)
            for j in range(TILES):
                last = pe.transpose(kept_ps[0][:, j * TILE:j * TILE + TILE], dense_rows[:, j, :], identity[:])
            last.then_inc(s_kept_ps, 1)

            def look_up(i):
                pe.wait_ge(s_high, i + 1)
                pe.wait_ge(s_low, i + 1)
                if i >= 1:
                    pe.wait_ge(s_kept, i)
                a = first_sample(i)
                out = kept_ps[(i + 1) % 2][:, a:]
                for c in range(CHUNKS):
                    pe.wait_ge(s_onehot, CHUNKS * i + c + 1)
                    pe.matmul(out, high[i % 2][:, c, :], onehot[i % 2][:, c, a:], start=(c == 0), stop=False)
                    last = pe.matmul(out, low[i % 2][:, c, :], onehot[i % 2][:, c, a:],
                                     start=False, stop=(c == CHUNKS - 1))
                last.then_inc(s_kept_ps, 1)

            def steps_of_tile(t, steps, first=False):
                for step, i in steps:
                    if step == "look":
                        look_up(i)
                    elif step == "turn":
                        turn_set(t, i, first)
                    elif step == "late":
                        turn_late(i)
                    elif step == "layer1":
                        layer1(t - 1)
                    elif step == "layer2":
                        layer2(t - 1)
                    elif step == "layer3":
                        layer3(t - 1)
                    elif step == "gram":
                        gram_tile(t, first)

            pe.wait_ge(s_gram_zero, 1)
            steps_of_tile(0, FIRST_STEPS, first=True)
            pe.wait_ge(s_w1, 16)
            pe.wait_ge(s_w2, 16)
            pe.wait_ge(s_w3, 16)
            steps_of_tile(1, SECOND_STEPS)
            pe.wait_ge(s_kept, KEPT)
            with pe.Fori(2, TILES) as t:
                steps_of_tile(t, TILE_STEPS)
            layer1_last(TILES - 1)
            layer2_last(TILES - 1)
            layer3(TILES - 1, last_tile=True)

        def set_columns(k):
            a = KEPT + SETS[k][0]
            return vectors[:, :, a:a + len(SETS[k])].rearrange("p b v -> p v b")

        def late_columns(j):
            a = 1 + EARLY + LATE_SETS[j][0]
            return vectors[:, :, a:a + len(LATE_SETS[j])].rearrange("p b v -> p v b")

        def move(copy, s, q, h):
            n, a = slab_columns(s), h * HALF
            return copy(pairs[s * QUAD:s * QUAD + VECTORS, 0:n, q * GROUPS + a:q * GROUPS + a + HALF],
                        folded[q * QUAD:q * QUAD + VECTORS, s:FOLDED:QUADS, a:a + HALF])

        ACT_MOVES = [(s, q) for s in range(QUADS) for q in (0, 1)]
        DVE_MOVES = [(s, q) for s in range(QUADS) for q in (2, 3)]

        @block.scalar
        def _(act):
            act.dma_start(dense_rows[:], dense.rearrange("(j p) d -> p j d", p=TILE)).then_inc(s_dense, 16)

            def take_set(t, k):
                act.wait_ge(s_turned, t * len(SETS) + k + 1)
                act.copy(set_columns(k), turned[k % 2][:, 0:len(SETS[k]), :]).then_inc(s_vec, 1)

            def take_kept(t, a, b):
                return act.copy(vectors[:, :, a:b].rearrange("p b v -> p v b"),
                                kept[:, a:b, bass.ds(t * TILE, TILE)])

            def move_pairs(t, first):
                if not first:
                    act.wait_ge(s_h1_ps, t)
                for h in range(2):
                    act.wait_ge(s_folded, 2 * t + (h + 1))
                    for s, q in ACT_MOVES:
                        last = move(act.copy, s, q, h)
                    last.then_inc(s_pairs_act, 1)

            def relu1(t):
                act.wait_ge(s_h1_ps, t + 1)
                act.activation(h1[:], h1_ps[:], ACT.Relu).then_inc(s_h1, 1)

            def relu2(t):
                act.wait_ge(s_h2_ps, t + 1)
                for c in range(CHUNKS2):
                    last = act.activation(h2[:, c, :], h2_ps[:, c, :], ACT.Relu, bias=b2_sb[:, c:c + 1])
                last.then_inc(s_h2, 1)

            def split_high(i):
                act.wait_ge(s_table[i], 16)
                if i >= 2:
                    act.wait_ge(s_kept_ps, i)
                act.copy(high[i % 2][:], table_sb[i][:]).then_inc(s_high, 1)

            def keep(v):
                act.wait_ge(s_kept_ps, v + 1)
                a = first_sample(v - 1)
                act.copy(kept[:, v, a:], kept_ps[v % 2][:, a:]).then_inc(s_kept, 1)

            split_high(0)
            split_high(1)
            keep(0)
            def steps_of_tile(t, steps, first=False):
                for step, i in steps:
                    if step == "look":
                        if i == LOOKUPS - 1:
                            act.wait_ge(s_kept, KEPT - 1)
                            act.wait_ge(s_gram, 2 * t)
                            take_kept(t, 0, KEPT - 1)
                        keep(i + 1)
                        if i + 2 < LOOKUPS:
                            split_high(i + 2)
                        if i == EARLY - 1:
                            act.wait_ge(s_kept, 1 + EARLY)
                            take_kept(t, 0, 1 + EARLY).then_inc(s_vec_kept, 1)
                        if i == LOOKUPS - 1:
                            act.wait_ge(s_kept, KEPT)
                            take_kept(t, KEPT - 1, KEPT).then_inc(s_vec_kept, 1)
                    elif step == "turn":
                        take_set(t, i)
                    elif step == "late":
                        act.wait_ge(s_late_turned, i + 1)
                        act.copy(late_columns(i), turned[(len(SETS) + i) % 2][:, 0:len(LATE_SETS[i]), :])\
                           .then_inc(s_late_vec, 1)
                    elif step == "layer1":
                        relu1(t - 1)
                    elif step == "layer2":
                        relu2(t - 1)
                    elif step == "gram":
                        if first:
                            act.dma_start(w1_sb[:], w1).then_inc(s_w1, 16)
                            act.dma_start(w2_sb[:], w2.rearrange("(k p) n -> p k n", p=128)).then_inc(s_w2, 16)
                            act.dma_start(b2_sb[:], b2).then_inc(s_b2, 16)
                            act.dma_start(w3_sb[:], w3).then_inc(s_w3, 16)
                    elif step == "fold":
                        move_pairs(t, first)

            act.wait_ge(s_pairs_init, 2)
            steps_of_tile(0, FIRST_STEPS, first=True)
            act.wait_ge(s_b2, 16)
            steps_of_tile(1, SECOND_STEPS)
            with act.Fori(2, TILES) as t:
                act.wait_ge(s_gram, 2 * t)
                take_kept(t, 0, KEPT).then_inc(s_vec_kept, 1)
                steps_of_tile(t, TILE_STEPS)
            for c in range(CHUNKS1):
                act.wait_ge(s_h1_last_ps, c + 1)
                act.activation(h1[:, c, :], layer1_last_ps[c], ACT.Relu).then_inc(s_h1, 1)
            for c in range(CHUNKS2):
                act.wait_ge(s_h2_last_ps, c + 1)
                act.activation(h2[:, c, :], layer2_last_ps[c], ACT.Relu, bias=b2_sb[:, c:c + 1]).then_inc(s_h2, 1)

        @block.vector
        def _(dve):
            dve.memset(gram[:], 0.0).then_inc(s_gram_zero, 1)

            def fold(t, h, first):
                dve.wait_ge(s_gram, 2 * t + (h + 1))
                if not first:
                    dve.wait_ge(s_pairs_act, 2 * t)
                half = folded[:, :, h * HALF:h * HALF + HALF]
                columns = gram[:, h].rearrange("p g c -> p c g")
                dve.tensor_copy(half, columns[:, HALF_CYCLE:VECTORS]).then_inc(s_far, 1)
                dve.wait_ge(s_mask, 16)
                dve.wait_ge(s_far, 2 * t + (h + 1))
                dve.copy_predicated(half[:, 0:HALF_CYCLE],
                                    keep_low_sb[:].unsqueeze(2).to_broadcast([128, HALF_CYCLE, HALF]),
                                    columns[:, 0:HALF_CYCLE]).then_inc(s_folded, 1)

            def move_pairs(t, h, first):
                dve.wait_ge(s_folded, 2 * t + (h + 1))
                if not first:
                    dve.wait_ge(s_h1_ps, t)
                for s, q in DVE_MOVES:
                    last = move(dve.tensor_copy, s, q, h)
                last.then_inc(s_pairs_dve, 1)

            def take_y(t):
                dve.wait_ge(s_y_ps, t + 1)
                dve.tensor_copy(y_sb[:, bass.ds(t * TILE, TILE)], y_ps).then_inc(s_y, 1)

            def split_low(i):
                dve.wait_ge(s_high, i + 1)
                if i >= 2:
                    dve.wait_ge(s_kept_ps, i)
                dve.tensor_tensor(low[i % 2][:], table_sb[i][:], high[i % 2][:].bitcast(fp32), ALU.subtract)\
                   .then_inc(s_low, 1)

            def one_hot(i):
                dve.wait_ge(s_lookup_ids[i], 16)
                a = first_sample(i)
                for c in range(CHUNKS):
                    dve.tensor_scalar(onehot[i % 2][:, c, a:], ids_sb[i][:, a:], row_ids_sb[:, c:c + 1], None,
                                      ALU.is_equal).then_inc(s_onehot, 1)

            dve.wait_ge(s_row_ids, 16)
            def steps_of_tile(t, steps, first=False):
                for step, i in steps:
                    if step == "look":
                        split_low(i)
                        one_hot(i)
                    elif step == "layer3":
                        take_y(t - 1)
                    elif step == "fold":
                        for h in range(2):
                            fold(t, h, first)
                            move_pairs(t, h, first)

            dve.wait_ge(s_pairs_init, 2)
            steps_of_tile(0, FIRST_STEPS, first=True)
            steps_of_tile(1, SECOND_STEPS)
            with dve.Fori(2, TILES) as t:
                steps_of_tile(t, TILE_STEPS)
            take_y(TILES - 1)


def kernel(**inputs):
    import numpy as np
    import concourse.bacc as bacc
    from concourse.bass_utils import run_bass_kernel_spmd

    w_top1 = np.asarray(inputs["W_top1"])
    w1 = np.zeros((128, K1, HIDDEN1), w_top1.dtype)
    keep_low = np.zeros((128, HALF_CYCLE), np.int32)
    for c in range(FOLDED):
        s, k = c % QUADS, c // QUADS
        for n in range(VECTORS):
            for m in (c, c + HALF_CYCLE):
                if c == HALF_CYCLE and m == c:
                    continue
                if 1 <= (m - n) % VECTORS <= HALF_CYCLE:
                    a, b = sorted((ORDER[n], ORDER[m]))
                    w1[s * QUAD + n, k] = w_top1[a * VECTORS - a * (a + 1) // 2 + b - a - 1]
                    if m == c:
                        for q in range(QUADS):
                            keep_low[q * QUAD + n, c] = 1
    w1[VECTORS, 0] = np.asarray(inputs["b_top1"])
    w1[:, SLABS] = w_top1[PAIRS:]

    arrays = {
        "dense": np.asarray(inputs["r_dense"]),
        "ids": np.ascontiguousarray(np.asarray(inputs["ids"])[:, GATHERED].reshape(TILES, TILE, NG)),
        "lookup_ids": np.ascontiguousarray(np.asarray(inputs["ids"])[:, LOOKED_UP].T),
        "late_ids": np.ascontiguousarray(np.asarray(inputs["ids"])[:TILE, LOOKED_UP[EARLY:]]),
        "row_ids": np.arange(TABLE_PARTS * CHUNKS, dtype=np.float32).reshape(TABLE_PARTS, CHUNKS),
        "w1": w1,
        "w2": np.asarray(inputs["W_top2"]),
        "b2": np.ascontiguousarray(np.asarray(inputs["b_top2"]).reshape(CHUNKS2, 128).T),
        "w3": np.ascontiguousarray(np.asarray(inputs["W_top3"]).reshape(CHUNKS2, 128).T),
        "keep_low": keep_low,
    }
    for f in range(TABLES):
        arrays[f"table{f}"] = np.asarray(inputs[f"tbl_{f}"])

    nc = bacc.Bacc("TRN2", target_bir_lowering=False, num_devices=1)
    ins = {n: nc.dram_tensor(n, a.shape, mybir.dt.from_np(a.dtype), kind="ExternalInput").ap()
           for n, a in arrays.items()}
    y = nc.dram_tensor("y", (BATCH, 1), mybir.dt.float32, kind="ExternalOutput").ap()
    build(nc, ins["dense"], ins["ids"], ins["lookup_ids"], ins["late_ids"], ins["row_ids"], [ins[f"table{f}"] for f in range(TABLES)],
          ins["w1"], ins["w2"], ins["b2"], ins["w3"], ins["keep_low"], y)
    return run_bass_kernel_spmd(nc, [arrays], core_ids=[0]).results[0]["y"]
```

```python
import concourse.bass as bass
from concourse import mybir
from contextlib import ExitStack

BATCH = 512
TABLES = 26
DIM = 128
VECTORS = TABLES + 1
HIDDEN1, HIDDEN2 = 512, 256
PAIRS = VECTORS * (VECTORS - 1) // 2

TILE = 128
TILES = BATCH // TILE
QUADS = 4
QUAD = 32
GROUPS = TILE // QUADS
HALF = GROUPS // 2
HALF_CYCLE = (VECTORS - 1) // 2
FOLDED = HALF_CYCLE + 1
SLABS = -(-FOLDED // QUADS)
K1 = SLABS + 1
CHUNKS1, CHUNKS2 = HIDDEN1 // 128, HIDDEN2 // 128

ROWS = [125000, 12500, 1000, 12500, 1000, 12500, 12500, 12500, 1000, 1000, 12500, 12500, 12500, 12500,
        1000, 1000, 1250, 1250, 1250, 1000, 1000, 1250, 1000, 1000, 1000, 1000]
EARLY, LATE = 3, 8
LOOKUPS = EARLY + LATE
LOOKED_UP = [f for f in range(TABLES) if ROWS[f] == min(ROWS)][:LOOKUPS]
GATHERED = [f for f in range(TABLES) if f not in LOOKED_UP]
NG = len(GATHERED)
LOAD_AHEAD = 3
W1_AFTER, W2_AFTER = 8, 10
IDS_AFTER = [4, 6]
WARM_UP = 20
CHUNKS = 8
TABLE_PARTS = min(ROWS) // CHUNKS
DVE_CHUNKS = 7
ORDER = [0] + [f + 1 for f in LOOKED_UP + GATHERED]
LAYER1_PARTS = [(0, 1), (2,), (3,)]
KEPT = 1 + LOOKUPS
GROUP = 4
SETS = [list(range(a, min(a + GROUP, NG))) for a in range(0, NG, GROUP)]
LATE_SETS = [list(range(a, min(a + GROUP, LATE))) for a in range(0, LATE, GROUP)]
ID_CUT = GROUP * (len(SETS) // 2)
ID_PARTS = [(0, ID_CUT), (ID_CUT, NG)]

TILE_STEPS = [("turn", 0), ("turn", 1), ("layer2", 0), ("kept", 0), ("layer1", 0), ("turn", 2), ("layer1", 1),
              ("turn", 3), ("layer1", 2), ("gram", 0), ("layer3", 0), ("gram", 1), ("fold", 0), ("move", 0)]
FIRST_STEPS = [("look", 0), ("turn", 0), ("split", 2),
               ("look", 1), ("turn", 1), ("split", 3),
               ("look", 2), ("turn", 2), ("split", 4),
               ("look", 3), ("turn", 3), ("split", 5),
               ("look", 4), ("late", 0), ("split", 6),
               ("look", 5), ("split", 7), ("late", 1),
               ("look", 6), ("split", 8), ("busy", 4), ("gram", 0), ("gram", 1), ("move", 0),
               ("look", 7), ("fold", 0)]
SECOND_STEPS = [("split", 9), ("layer1", 0), ("turn", 0),
                ("look", 8), ("turn", 1), ("split", 10),
                ("look", 9), ("turn", 2),
                ("look", 10), ("turn", 3), ("layer1", 1), ("layer1", 2), ("gram", 0), ("gram", 1), ("fold", 0),
                ("move", 0)]
assert [i for step, i in FIRST_STEPS + SECOND_STEPS if step == "look"] == list(range(LOOKUPS))
assert [i for step, i in FIRST_STEPS if step == "late"] == list(range(len(LATE_SETS)))
for steps in (TILE_STEPS, FIRST_STEPS, SECOND_STEPS):
    assert [i for step, i in steps if step == "turn"] == list(range(len(SETS)))
assert W1_AFTER < W2_AFTER < LOOKUPS and max(IDS_AFTER) < LOOKUPS


def first_sample(i):
    return 0 if i < EARLY else TILE


def slab_columns(s):
    return (FOLDED - s + QUADS - 1) // QUADS


def build(nc, dense, ids, lookup_ids, late_ids, row_ids, tables, w1, w2, b2, w3, keep_low, y):
    fp32, fp32r, i32 = mybir.dt.float32, mybir.dt.float32r, mybir.dt.int32
    ALU = mybir.AluOpType
    ACT = mybir.ActivationFunctionType

    with ExitStack() as ctx:
        def sb(name, shape, dt=fp32):
            return ctx.enter_context(nc.sbuf_tensor(name, shape, dt))

        def ps(name, shape):
            return ctx.enter_context(nc.psum_tensor(name, shape, fp32))

        def sem(name):
            return ctx.enter_context(nc.semaphore(name))

        identity = sb("identity", [128, 128])
        id_part = [sb(f"id_part{h}", [TILE, b - a], i32) for h, (a, b) in enumerate(ID_PARTS)]
        dense_rows = sb("dense_rows", [TILE, TILES, DIM])
        row_ids_sb = sb("row_ids_sb", [TABLE_PARTS, 2, CHUNKS])
        distance = sb("distance", [TABLE_PARTS, CHUNKS - DVE_CHUNKS, BATCH])
        table_sb = [sb(f"table_sb{i}", [TABLE_PARTS, CHUNKS, DIM]) for i in range(LOOKUPS)]
        ids_sb = [sb(f"ids_sb{i}", [TABLE_PARTS, BATCH], i32) for i in range(LOOKUPS)]
        high = [sb(f"high{i}", [TABLE_PARTS, CHUNKS, DIM], fp32r) for i in range(2)]
        low = [sb(f"low{i}", [TABLE_PARTS, CHUNKS, DIM], fp32r) for i in range(2)]
        onehot = [sb(f"onehot{i}", [TABLE_PARTS, CHUNKS, BATCH], fp32r) for i in range(2)]
        late_id_sb = sb("late_id_sb", [TILE, LATE], i32)
        late_rows = sb("late_rows", [TILE, LATE, DIM])
        rows = sb("rows", [TILE, NG, DIM])
        kept = sb("kept", [DIM, KEPT, BATCH])
        vectors = sb("vectors", [DIM, TILE, VECTORS])
        folded = sb("folded", [128, FOLDED, GROUPS])
        pairs = sb("pairs", [128, SLABS, TILE])
        keep_low_sb = sb("keep_low_sb", [128, FOLDED - 1], i32)
        w1_sb = sb("w1_sb", [128, K1, HIDDEN1])
        w2_sb = sb("w2_sb", [128, CHUNKS1, HIDDEN2])
        b2_sb = sb("b2_sb", [128, CHUNKS2])
        w3_sb = sb("w3_sb", [128, CHUNKS2])
        h1 = sb("h1", [128, CHUNKS1, TILE])
        h2 = sb("h2", [128, CHUNKS2, TILE])
        y_sb = sb("y_sb", [1, BATCH])

        turned = [ps(f"turned{i}", [DIM, GROUP, TILE]) for i in range(2)]
        gram = ps("gram", [128, 2, HALF, 32])
        kept_ps = [ps(f"kept_ps{i}", [DIM, BATCH]) for i in range(2)]
        h1_ps = ps("h1_ps", [128, 4, TILE])
        h2_ps = ps("h2_ps", [128, 4, TILE])
        layer1_last_ps = [h1_ps[:, 0, :], turned[0][:, 0, :], turned[1][:, 0, :], kept_ps[0][:, 0:TILE]]
        layer2_last_ps = [kept_ps[1][:, 0:TILE], h2_ps[:, 0, :]]
        y_ps = kept_ps[1][0:1, TILE:2 * TILE]

        s_ids = [sem(f"s_ids{h}") for h in range(2)]
        s_dense = sem("s_dense")
        s_mask = sem("s_mask")
        s_w1 = sem("s_w1")
        s_w2 = sem("s_w2")
        s_b2 = sem("s_b2")
        s_w3 = sem("s_w3")
        s_out = sem("s_out")
        s_gathered = [sem(f"s_gathered{k}") for k in range(len(SETS))]
        s_identity = sem("s_identity")
        s_pairs_init = sem("s_pairs_init")
        s_gram_zero = sem("s_gram_zero")
        s_row_ids = sem("s_row_ids")
        s_late_ids = sem("s_late_ids")
        s_late_gathered = [sem(f"s_late_gathered{j}") for j in range(len(LATE_SETS))]
        s_late_turned = sem("s_late_turned")
        s_late_vec = sem("s_late_vec")
        s_table = [sem(f"s_table{i}") for i in range(LOOKUPS)]
        s_lookup_ids = [sem(f"s_lookup_ids{i}") for i in range(LOOKUPS)]
        s_high = sem("s_high")
        s_low = sem("s_low")
        s_onehot = sem("s_onehot")
        s_distance = sem("s_distance")
        s_onehot_act = sem("s_onehot_act")
        s_kept_ps = sem("s_kept_ps")
        s_kept = sem("s_kept")
        s_turned = sem("s_turned")
        s_vec = sem("s_vec")
        s_vec_kept = sem("s_vec_kept")
        s_gram = sem("s_gram")
        s_far = sem("s_far")
        s_folded = sem("s_folded")
        s_pairs_act = sem("s_pairs_act")
        s_pairs_dve = sem("s_pairs_dve")
        s_h1_ps = sem("s_h1_ps")
        s_h1_last_ps = sem("s_h1_last_ps")
        s_h2_last_ps = sem("s_h2_last_ps")
        s_h1 = sem("s_h1")
        s_h2_ps = sem("s_h2_ps")
        s_h2 = sem("s_h2")
        s_y_ps = sem("s_y_ps")
        s_y = sem("s_y")

        block = ctx.enter_context(nc.Block())

        @block.sync
        def _(sp):
            def load_ids_of_tile0(h):
                a, b = ID_PARTS[h]
                sp.dma_start(id_part[h][:], ids[0, :, a:b]).then_inc(s_ids[h], 16)

            def load_table(i):
                a = first_sample(i)
                if i > 0:
                    sp.dma_start(ids_sb[i][:, a:], lookup_ids[i:i + 1, a:].partition_broadcast(TABLE_PARTS)
                                 .rearrange("p o b -> p (o b)")).then_inc(s_lookup_ids[i], 16)
                sp.dma_start(table_sb[i][:], tables[LOOKED_UP[i]].rearrange("(p c) d -> p c d", c=CHUNKS))\
                  .then_inc(s_table[i], 16)

            def load_ids_of_tile(t, h):
                a, b = ID_PARTS[h]
                sp.wait_ge(s_ids[h], 16)
                for k, members in enumerate(SETS):
                    if a <= members[0] < b:
                        sp.wait_ge(s_gathered[k], t * (16 * len(members)))
                sp.dma_start(id_part[h][:], ids[bass.ds(t, 1), :, a:b].rearrange("o p f -> (o p) f"))\
                  .then_inc(s_ids[h], 16)

            load_ids_of_tile0(0)
            sp.dma_start(row_ids_sb[:], row_ids).then_inc(s_row_ids, 16)
            load_table(0)
            sp.dma_start(dense_rows[:], dense.rearrange("(j p) d -> p j d", p=TILE)).then_inc(s_dense, 16)
            load_ids_of_tile0(1)
            sp.dma_start(late_id_sb[:], late_ids).then_inc(s_late_ids, 16)
            sp.dma_start(keep_low_sb[:], keep_low).then_inc(s_mask, 16)
            for i in range(1, LOOKUPS):
                if i >= LOAD_AHEAD:
                    sp.wait_ge(s_low, i - LOAD_AHEAD + 1)
                load_table(i)
                if i == W1_AFTER:
                    sp.wait_ge(s_late_gathered[-1], 16 * len(LATE_SETS[-1]))
                    sp.dma_start(w1_sb[:], w1).then_inc(s_w1, 16)
                if i == W2_AFTER:
                    sp.dma_start(w2_sb[:], w2.rearrange("(k p) n -> p k n", p=128)).then_inc(s_w2, 16)
                    sp.dma_start(b2_sb[:], b2).then_inc(s_b2, 16)
                    sp.dma_start(w3_sb[:], w3).then_inc(s_w3, 16)
                if i in IDS_AFTER:
                    load_ids_of_tile(1, IDS_AFTER.index(i))
            with sp.Fori(2, TILES) as t:
                for h in range(2):
                    load_ids_of_tile(t, h)
            sp.wait_ge(s_y, TILES)
            sp.dma_start(y.rearrange("b o -> o b"), y_sb[:]).then_inc(s_out, 16)
            sp.wait_ge(s_out, 16)

        @block.gpsimd
        def _(pool):
            pool.memset(identity[:], 0.0).then_inc(s_identity, 1)
            pool.wait_ge(s_identity, 1)
            pool.affine_select(out=identity[:], in_=identity[:], compare_op=ALU.not_equal, fill=1.0, base=0,
                               pattern=[[-1, 128]], channel_multiplier=1).then_inc(s_identity, 1)
            sets_read = pool.alloc_register("sets_read")
            pool.reg_mov(sets_read, 1)

            def gather_tile(t, first):
                for h, (a, b) in enumerate(ID_PARTS):
                    pool.wait_ge(s_ids[h], t * 16 + 16)
                    for k, members in enumerate(SETS):
                        if not a <= members[0] < b:
                            continue
                        if not first:
                            pool.wait_ge(s_turned, sets_read)
                            pool.reg_add(sets_read, sets_read, 1)
                        for g in members:
                            pool.indirect_dma_start(rows[:, g, :], None, tables[GATHERED[g]],
                                                    bass.IndirectOffsetOnAxis(id_part[h][:, g - a:g - a + 1], 0))\
                                .then_inc(s_gathered[k], 16)

            gather_tile(0, first=True)
            pool.wait_ge(s_late_ids, 16)
            for j, members in enumerate(LATE_SETS):
                for g in members:
                    pool.indirect_dma_start(late_rows[:, g, :], None, tables[LOOKED_UP[EARLY + g]],
                                            bass.IndirectOffsetOnAxis(late_id_sb[:, g:g + 1], 0))\
                        .then_inc(s_late_gathered[j], 16)
            with pool.Fori(1, TILES) as t:
                gather_tile(t, first=False)

        @block.tensor
        def _(pe):
            def turn_set(t, k, first):
                members = SETS[k]
                pe.wait_ge(s_gathered[k], t * (16 * len(members)) + 16 * len(members))
                if not first or k >= 2:
                    pe.wait_ge(s_vec, t * len(SETS) + (k - 1))
                for i, g in enumerate(members):
                    last = pe.transpose(turned[k % 2][:, i, :], rows[:, g, :], identity[:])
                last.then_inc(s_turned, 1)

            def turn_late(j):
                pe.wait_ge(s_late_gathered[j], 16 * len(LATE_SETS[j]))
                n = len(SETS) + j
                pe.wait_ge(s_vec, len(SETS))
                if j >= 2:
                    pe.wait_ge(s_late_vec, j - 1)
                for i, g in enumerate(LATE_SETS[j]):
                    last = pe.transpose(turned[n % 2][:, i, :], late_rows[:, g, :], identity[:])
                last.then_inc(s_late_turned, 1)

            def pairs_ready(t, h):
                pe.wait_ge(s_pairs_act, 2 * t + (h + 1))
                pe.wait_ge(s_pairs_dve, 2 * t + (h + 1))

            def layer1(t, part):
                for c in LAYER1_PARTS[part]:
                    pe.matmul(h1_ps[:, c, :], w1_sb[:, SLABS, c * 128:c * 128 + 128],
                              kept[:, 0, bass.ds(t * TILE, TILE)], start=True, stop=False)
                    if c == 0:
                        pairs_ready(t, 1)
                    for k in range(SLABS):
                        last = pe.matmul(h1_ps[:, c, :], w1_sb[:, k, c * 128:c * 128 + 128], pairs[:, k, :],
                                         start=False, stop=(k == SLABS - 1))
                if part == len(LAYER1_PARTS) - 1:
                    last.then_inc(s_h1_ps, 1)

            def layers_last(t):
                outs = [layer1_last_ps[c] for c in range(CHUNKS1)]
                layer2(t - 1)
                pe.wait_ge(s_vec, TILES * len(SETS))
                for c in range(CHUNKS1):
                    pe.matmul(outs[c], w1_sb[:, SLABS, c * 128:c * 128 + 128],
                              kept[:, 0, t * TILE:t * TILE + TILE], start=True, stop=False)
                pairs_ready(t, 1)
                for c in range(CHUNKS1):
                    for k in range(SLABS):
                        last = pe.matmul(outs[c], w1_sb[:, k, c * 128:c * 128 + 128],
                                         pairs[:, k, :],
                                         start=False, stop=(k == SLABS - 1))
                    last.then_inc(s_h1_last_ps, 1)
                    if c == 1:
                        layer3(t - 1)
                layer2_last(t)
                layer3(t, last_tile=True)

            def layer2(t):
                pe.wait_ge(s_h1, t + 1)
                for c in range(CHUNKS2):
                    for k in range(CHUNKS1):
                        last = pe.matmul(h2_ps[:, c, :], w2_sb[:, k, c * 128:c * 128 + 128], h1[:, k, :],
                                         start=(k == 0), stop=(k == CHUNKS1 - 1))
                last.then_inc(s_h2_ps, 1)

            def layer2_last(t):
                pe.wait_ge(s_y, t)
                for c in range(CHUNKS2):
                    for k in range(CHUNKS1):
                        if c == 0:
                            pe.wait_ge(s_h1, t + (k + 1))
                        last = pe.matmul(layer2_last_ps[c], w2_sb[:, k, c * 128:c * 128 + 128], h1[:, k, :],
                                         start=(k == 0), stop=(k == CHUNKS1 - 1))
                    last.then_inc(s_h2_last_ps, 1)

            def layer3(t, last_tile=False):
                if not last_tile:
                    pe.wait_ge(s_h2, t + 1)
                for k in range(CHUNKS2):
                    if last_tile:
                        pe.wait_ge(s_h2, t + (k + 1))
                    last = pe.matmul(y_ps, w3_sb[:, k:k + 1], h2[:, k, :], start=(k == 0), stop=(k == CHUNKS2 - 1))
                last.then_inc(s_y_ps, 1)

            def gram_half(t, h, first):
                if h == 0:
                    pe.wait_ge(s_vec, t * len(SETS) + len(SETS))
                    pe.wait_ge(s_vec_kept, t + 1)
                    if first:
                        pe.wait_ge(s_late_vec, len(LATE_SETS))
                if not first:
                    pe.wait_ge(s_folded, 2 * t + (h - 1))
                for g in range(HALF):
                    for q in range(QUADS):
                        v = vectors[:, q * GROUPS + h * HALF + g, :]
                        last = pe.matmul(gram[q * QUAD:q * QUAD + VECTORS, h, g, 0:VECTORS], v, v,
                                         start=True, stop=True)
                last.then_inc(s_gram, 1)

            def keep_busy(n):
                for j in range(n):
                    pe.transpose(h1_ps[:, j % 4, :], identity[:], identity[:])

            pe.wait_ge(s_identity, 2)
            keep_busy(WARM_UP)
            pe.wait_ge(s_dense, 16)
            for j in range(TILES):
                last = pe.transpose(kept_ps[0][:, j * TILE:j * TILE + TILE], dense_rows[:, j, :], identity[:])
            last.then_inc(s_kept_ps, 1)

            def look_up(i):
                pe.wait_ge(s_high, i + 1)
                if i >= 1:
                    pe.wait_ge(s_kept, i)
                a = first_sample(i)
                out = kept_ps[(i + 1) % 2][:, a:]
                for c in range(CHUNKS):
                    if c < DVE_CHUNKS:
                        pe.wait_ge(s_onehot, DVE_CHUNKS * i + c + 1)
                    else:
                        pe.wait_ge(s_onehot_act, i + 1)
                    pe.matmul(out, high[i % 2][:, c, :], onehot[i % 2][:, c, a:], start=(c == 0), stop=False)
                pe.wait_ge(s_low, i + 1)
                for c in range(CHUNKS):
                    last = pe.matmul(out, low[i % 2][:, c, :], onehot[i % 2][:, c, a:],
                                     start=False, stop=(c == CHUNKS - 1))
                last.then_inc(s_kept_ps, 1)

            def steps_of_tile(t, steps, first=False, second=False):
                for step, i in steps:
                    if step == "look":
                        look_up(i)
                    elif step == "turn":
                        turn_set(t, i, first)
                    elif step == "late":
                        turn_late(i)
                    elif step == "layer1":
                        if second and i == 0:
                            pe.wait_ge(s_w1, 16)
                        layer1(t - 1, i)
                    elif step == "layer2":
                        layer2(t - 2)
                    elif step == "layer3":
                        layer3(t - 2)
                    elif step == "gram":
                        gram_half(t, i, first)
                    elif step == "busy":
                        keep_busy(i)

            pe.wait_ge(s_gram_zero, 1)
            steps_of_tile(0, FIRST_STEPS, first=True)
            steps_of_tile(1, SECOND_STEPS, second=True)
            pe.wait_ge(s_w2, 16)
            pe.wait_ge(s_w3, 16)
            pe.wait_ge(s_kept, KEPT)
            with pe.Fori(2, TILES) as t:
                steps_of_tile(t, TILE_STEPS)
            layers_last(TILES - 1)

        def set_columns(k):
            a = KEPT + SETS[k][0]
            return vectors[:, :, a:a + len(SETS[k])].rearrange("p b v -> p v b")

        def late_columns(j):
            a = 1 + EARLY + LATE_SETS[j][0]
            return vectors[:, :, a:a + len(LATE_SETS[j])].rearrange("p b v -> p v b")

        def move(copy, s, q, h):
            n, a = slab_columns(s), h * HALF
            return copy(pairs[s * QUAD:s * QUAD + VECTORS, 0:n, q * GROUPS + a:q * GROUPS + a + HALF],
                        folded[q * QUAD:q * QUAD + VECTORS, s:FOLDED:QUADS, a:a + HALF])

        ACT_MOVES = [(s, q) for s in range(QUADS) for q in (0, 1)]
        DVE_MOVES = [(s, q) for s in range(QUADS) for q in (2, 3)]

        @block.scalar
        def _(act):
            act.dma_start(ids_sb[0][:], lookup_ids[0:1, :].partition_broadcast(TABLE_PARTS)
                          .rearrange("p o b -> p (o b)")).then_inc(s_lookup_ids[0], 16)
            act.wait_ge(s_identity, 2)
            act.activation(y_sb[:, 0:1], identity[0:1, 0:1], ACT.Abs)

            def take_set(t, k):
                act.wait_ge(s_turned, t * len(SETS) + k + 1)
                act.copy(set_columns(k), turned[k % 2][:, 0:len(SETS[k]), :]).then_inc(s_vec, 1)

            def take_kept(t, a, b):
                return act.copy(vectors[:, :, a:b].rearrange("p b v -> p v b"),
                                kept[:, a:b, bass.ds(t * TILE, TILE)])

            def move_pairs(t, first):
                if not first:
                    act.wait_ge(s_h1_ps, t)
                for h in range(2):
                    act.wait_ge(s_folded, 2 * t + (h + 1))
                    for s, q in ACT_MOVES:
                        last = move(act.copy, s, q, h)
                    last.then_inc(s_pairs_act, 1)

            def relu1(t):
                act.wait_ge(s_h1_ps, t + 1)
                act.activation(h1[:], h1_ps[:], ACT.Relu).then_inc(s_h1, 1)

            def relu2(t):
                act.wait_ge(s_h2_ps, t + 1)
                for c in range(CHUNKS2):
                    last = act.activation(h2[:, c, :], h2_ps[:, c, :], ACT.Relu, bias=b2_sb[:, c:c + 1])
                last.then_inc(s_h2, 1)

            def split_high(i):
                act.wait_ge(s_table[i], 16)
                if i >= 2:
                    act.wait_ge(s_kept_ps, i)
                act.copy(high[i % 2][:], table_sb[i][:]).then_inc(s_high, 1)

            def one_hot(i):
                act.wait_ge(s_row_ids, 16)
                act.wait_ge(s_lookup_ids[i], 16)
                if i >= 2:
                    act.wait_ge(s_kept_ps, i)
                if i >= 1:
                    act.wait_ge(s_onehot_act, i)
                a = first_sample(i)
                for c in range(DVE_CHUNKS, CHUNKS):
                    last = act.activation(distance[:, c - DVE_CHUNKS, a:], ids_sb[i][:, a:], ACT.Abs,
                                          bias=row_ids_sb[:, 1, c:c + 1])
                last.then_inc(s_distance, 1)
                act.wait_ge(s_distance, i + 1)
                act.activation(onehot[i % 2][:, DVE_CHUNKS:, a:], distance[:, :, a:], ACT.Relu, bias=1.0, scale=-1.0)\
                   .then_inc(s_onehot_act, 1)

            def keep(v):
                act.wait_ge(s_kept_ps, v + 1)
                a = first_sample(v - 1)
                act.copy(kept[:, v, a:], kept_ps[v % 2][:, a:]).then_inc(s_kept, 1)

            one_hot(0)
            split_high(0)
            one_hot(1)
            split_high(1)
            keep(0)
            def steps_of_tile(t, steps, first=False):
                for step, i in steps:
                    if step == "look":
                        if i == LOOKUPS - 1:
                            act.wait_ge(s_kept, KEPT - 1)
                            act.wait_ge(s_gram, 2 * t)
                            take_kept(t, 0, KEPT - 1)
                        keep(i + 1)
                        if i == EARLY - 1:
                            act.wait_ge(s_kept, 1 + EARLY)
                            take_kept(t, 0, 1 + EARLY).then_inc(s_vec_kept, 1)
                        if i == LOOKUPS - 1:
                            act.wait_ge(s_kept, KEPT)
                            take_kept(t, KEPT - 1, KEPT).then_inc(s_vec_kept, 1)
                    elif step == "split":
                        split_high(i)
                        one_hot(i)
                    elif step == "kept":
                        act.wait_ge(s_gram, 2 * t)
                        take_kept(t, 0, KEPT).then_inc(s_vec_kept, 1)
                    elif step == "turn":
                        take_set(t, i)
                    elif step == "late":
                        act.wait_ge(s_late_turned, i + 1)
                        act.copy(late_columns(i), turned[(len(SETS) + i) % 2][:, 0:len(LATE_SETS[i]), :])\
                           .then_inc(s_late_vec, 1)
                    elif step == "layer1":
                        if i == len(LAYER1_PARTS) - 1:
                            relu1(t - 1)
                    elif step == "layer2":
                        relu2(t - 2)
                    elif step == "move":
                        move_pairs(t, first)

            act.wait_ge(s_pairs_init, 1)
            steps_of_tile(0, FIRST_STEPS, first=True)
            steps_of_tile(1, SECOND_STEPS)
            act.wait_ge(s_b2, 16)
            with act.Fori(2, TILES) as t:
                steps_of_tile(t, TILE_STEPS)
            relu2(TILES - 2)
            for c in range(CHUNKS1):
                act.wait_ge(s_h1_last_ps, c + 1)
                act.activation(h1[:, c, :], layer1_last_ps[c], ACT.Relu).then_inc(s_h1, 1)
            for c in range(CHUNKS2):
                act.wait_ge(s_h2_last_ps, c + 1)
                act.activation(h2[:, c, :], layer2_last_ps[c], ACT.Relu, bias=b2_sb[:, c:c + 1]).then_inc(s_h2, 1)

        @block.vector
        def _(dve):
            dve.memset(gram[:], 0.0).then_inc(s_gram_zero, 1)
            dve.memset(pairs[:], 1.0).then_inc(s_pairs_init, 1)

            def fold(t, h, first):
                dve.wait_ge(s_gram, 2 * t + (h + 1))
                if not first:
                    dve.wait_ge(s_pairs_act, 2 * t)
                half = folded[:, :, h * HALF:h * HALF + HALF]
                columns = gram[:, h].rearrange("p g c -> p c g")
                dve.tensor_copy(half, columns[:, HALF_CYCLE:VECTORS]).then_inc(s_far, 1)
                dve.wait_ge(s_mask, 16)
                dve.wait_ge(s_far, 2 * t + (h + 1))
                dve.copy_predicated(half[:, 0:HALF_CYCLE],
                                    keep_low_sb[:].unsqueeze(2).to_broadcast([128, HALF_CYCLE, HALF]),
                                    columns[:, 0:HALF_CYCLE]).then_inc(s_folded, 1)

            def move_pairs(t, h, first):
                dve.wait_ge(s_folded, 2 * t + (h + 1))
                if not first:
                    dve.wait_ge(s_h1_ps, t)
                for s, q in DVE_MOVES:
                    last = move(dve.tensor_copy, s, q, h)
                last.then_inc(s_pairs_dve, 1)

            def take_y(t):
                dve.wait_ge(s_y_ps, t + 1)
                dve.tensor_copy(y_sb[:, bass.ds(t * TILE, TILE)], y_ps).then_inc(s_y, 1)

            def split_low(i):
                dve.wait_ge(s_high, i + 1)
                dve.tensor_tensor(low[i % 2][:], table_sb[i][:], high[i % 2][:].bitcast(fp32), ALU.subtract)\
                   .then_inc(s_low, 1)

            def one_hot(i):
                dve.wait_ge(s_lookup_ids[i], 16)
                if i >= 2:
                    dve.wait_ge(s_kept_ps, i)
                a = first_sample(i)
                for c in range(DVE_CHUNKS):
                    dve.tensor_scalar(onehot[i % 2][:, c, a:], ids_sb[i][:, a:], row_ids_sb[:, 0, c:c + 1], None,
                                      ALU.is_equal).then_inc(s_onehot, 1)

            dve.wait_ge(s_row_ids, 16)
            def steps_of_tile(t, steps, first=False):
                for step, i in steps:
                    if step == "look":
                        one_hot(i)
                        split_low(i)
                    elif step == "layer3":
                        take_y(t - 2)
                    elif step == "fold":
                        for h in range(2):
                            fold(t, h, first)
                            move_pairs(t, h, first)

            dve.wait_ge(s_pairs_init, 1)
            steps_of_tile(0, FIRST_STEPS, first=True)
            steps_of_tile(1, SECOND_STEPS)
            with dve.Fori(2, TILES) as t:
                steps_of_tile(t, TILE_STEPS)
            take_y(TILES - 2)
            take_y(TILES - 1)


def kernel(**inputs):
    import numpy as np
    import concourse.bacc as bacc
    from concourse.bass_utils import run_bass_kernel_spmd

    w_top1 = np.asarray(inputs["W_top1"])
    w1 = np.zeros((128, K1, HIDDEN1), w_top1.dtype)
    keep_low = np.zeros((128, HALF_CYCLE), np.int32)
    for c in range(FOLDED):
        s, k = c % QUADS, c // QUADS
        for n in range(VECTORS):
            for m in (c, c + HALF_CYCLE):
                if c == HALF_CYCLE and m == c:
                    continue
                if 1 <= (m - n) % VECTORS <= HALF_CYCLE:
                    a, b = sorted((ORDER[n], ORDER[m]))
                    w1[s * QUAD + n, k] = w_top1[a * VECTORS - a * (a + 1) // 2 + b - a - 1]
                    if m == c:
                        for q in range(QUADS):
                            keep_low[q * QUAD + n, c] = 1
    w1[VECTORS, 0] = np.asarray(inputs["b_top1"])
    w1[:, SLABS] = w_top1[PAIRS:]

    row_ids = np.arange(TABLE_PARTS * CHUNKS, dtype=np.float32).reshape(TABLE_PARTS, CHUNKS)
    arrays = {
        "dense": np.asarray(inputs["r_dense"]),
        "ids": np.ascontiguousarray(np.asarray(inputs["ids"])[:, GATHERED].reshape(TILES, TILE, NG)),
        "lookup_ids": np.ascontiguousarray(np.asarray(inputs["ids"])[:, LOOKED_UP].T),
        "late_ids": np.ascontiguousarray(np.asarray(inputs["ids"])[:TILE, LOOKED_UP[EARLY:]]),
        "row_ids": np.stack([row_ids, -row_ids], 1),
        "w1": w1,
        "w2": np.asarray(inputs["W_top2"]),
        "b2": np.ascontiguousarray(np.asarray(inputs["b_top2"]).reshape(CHUNKS2, 128).T),
        "w3": np.ascontiguousarray(np.asarray(inputs["W_top3"]).reshape(CHUNKS2, 128).T),
        "keep_low": keep_low,
    }
    for f in range(TABLES):
        arrays[f"table{f}"] = np.asarray(inputs[f"tbl_{f}"])

    nc = bacc.Bacc("TRN2", target_bir_lowering=False, num_devices=1)
    ins = {n: nc.dram_tensor(n, a.shape, mybir.dt.from_np(a.dtype), kind="ExternalInput").ap()
           for n, a in arrays.items()}
    y = nc.dram_tensor("y", (BATCH, 1), mybir.dt.float32, kind="ExternalOutput").ap()
    build(nc, ins["dense"], ins["ids"], ins["lookup_ids"], ins["late_ids"], ins["row_ids"],
          [ins[f"table{f}"] for f in range(TABLES)],
          ins["w1"], ins["w2"], ins["b2"], ins["w3"], ins["keep_low"], y)
    return run_bass_kernel_spmd(nc, [arrays], core_ids=[0]).results[0]["y"]
```
